# Optimizing a Trainium2 kernel written in Bass

```python
import numpy as np
import jax
import jax.numpy as jnp

def _softmax(x, axis=-1):
    return jax.nn.softmax(x, axis=axis)
def _gelu(x):
    return jax.nn.gelu(x, approximate=True)
def _silu(x):
    return jax.nn.silu(x)
def _sigmoid(x):
    return jax.nn.sigmoid(x)
def _layernorm(x, axis=-1, eps=1e-5):
    m = jnp.mean(x, axis=axis, keepdims=True)
    v = jnp.var(x, axis=axis, keepdims=True)
    return (x - m) / jnp.sqrt(v + eps)
def _scatter_add(tgt, idx, src, axis=0):
    return tgt.at[idx].add(src)
def _segment_sum(src, seg, n):
    return jax.ops.segment_sum(src, seg, n)

kernel_name = 'mk_conv_preact_d4_conv_nhwc32_db3b4f'

def setup_inputs(seed: int = 0):
    np.random.seed(seed)
    _w = jnp.asarray
    def _rec_inputs():
        import jax
        import jax.numpy as jnp
        _gk = jax.random.key(seed)
        x = -0.0001636 + 1 * jax.random.normal(jax.random.fold_in(_gk, 1), (16, 224, 224, 32), jnp.float32)
        return x
    x = _rec_inputs()
    def _L0_conv_setup():
        import jax, jax.numpy as jnp
        import numpy as np
        MAX_OFFSET = 28
        key = jax.random.key(seed)
        k1, k2, k3 = jax.random.split(key, 3)
        B, H, Wd, C = (64, 224, 224, 32)
        x = jax.random.normal(k1, (B, H, Wd, C), dtype=jnp.float32)
        W = jax.random.normal(k2, (C, 2), dtype=jnp.float32)
        b = jax.random.normal(k3, (2,), dtype=jnp.float32)
        return {'x': x, 'W': W, 'b': b, 'y': 224}
    _L0_conv_all = _L0_conv_setup()
    _L0_conv_in = {k: v for k, v in _L0_conv_all.items() if k in ('W', 'b', )}
    del _L0_conv_all

    def _L1_conv_setup():
        import jax, jax.numpy as jnp
        from jax import lax
        import numpy as np

        @jax.custom_vjp
        def ste_sign(x):
            return jnp.where(x >= 0, 1.0, -1.0).astype(x.dtype)

        def _ste_fwd(x):
            return (ste_sign(x), x)

        def _ste_bwd(x, g):
            return (g * (jnp.abs(x) <= 1.0).astype(g.dtype),)
        ste_sign.defvjp(_ste_fwd, _ste_bwd)
        key = jax.random.key(seed)
        k1, k2 = jax.random.split(key)
        B, H, Wd, Cin = (16, 256, 256, 32)
        M, kh, kw, Cout = (4, 3, 3, 32)
        x = jax.random.normal(k1, (B, H, Wd, Cin), dtype=jnp.float32)
        W = jax.random.normal(k2, (M, kh, kw, Cin, Cout), dtype=jnp.float32)
        b = jnp.zeros((M, Cout), dtype=jnp.float32)
        return {'x': x, 'W': W, 'b': b}
    _L1_conv_all = _L1_conv_setup()
    _L1_conv_in = {k: v for k, v in _L1_conv_all.items() if k in ('W', 'b', )}
    del _L1_conv_all

    def _L2_conv_setup():
        import jax, jax.numpy as jnp
        import numpy as np
        KX = 32
        KY = 32

        def dct_matrix(N):
            n = jnp.arange(N, dtype=jnp.float32)
            k = n[:, None]
            D = jnp.cos(jnp.pi * (n[None, :] + 0.5) * k / N)
            scale = jnp.where(jnp.arange(N) == 0, jnp.sqrt(1.0 / N), jnp.sqrt(2.0 / N))
            return (D * scale[:, None]).astype(jnp.float32)
        key = jax.random.key(seed)
        ks = jax.random.split(key, 5)
        B, nX, nY, dv = (16, 256, 256, 32)
        x = jax.random.normal(ks[0], (B, nX, nY, dv), dtype=jnp.float32)
        R_real = jax.random.uniform(ks[1], (KX, KY, dv, dv), dtype=jnp.float32)
        R_imag = jax.random.uniform(ks[2], (KX, KY, dv, dv), dtype=jnp.float32)
        W = jax.random.normal(ks[3], (dv, dv), dtype=jnp.float32) * (1.0 / np.sqrt(dv))
        b = jax.random.normal(ks[4], (dv,), dtype=jnp.float32) * 0.05
        return {'x': x, 'R_real': R_real, 'R_imag': R_imag, 'W': W, 'b': b}
    _L2_conv_all = _L2_conv_setup()
    _L2_conv_in = {k: v for k, v in _L2_conv_all.items() if k in ('R_real', 'R_imag', 'W', 'b', )}
    del _L2_conv_all

    def _L3_conv_setup():
        import jax, jax.numpy as jnp
        import numpy as np
        KX = 32
        KY = 32

        def dct_matrix(N):
            n = jnp.arange(N, dtype=jnp.float32)
            k = n[:, None]
            D = jnp.cos(jnp.pi * (n[None, :] + 0.5) * k / N)
            scale = jnp.where(jnp.arange(N) == 0, jnp.sqrt(1.0 / N), jnp.sqrt(2.0 / N))
            return (D * scale[:, None]).astype(jnp.float32)
        key = jax.random.key(seed)
        ks = jax.random.split(key, 5)
        B, nX, nY, dv = (16, 256, 256, 32)
        x = jax.random.normal(ks[0], (B, nX, nY, dv), dtype=jnp.float32)
        R_real = jax.random.uniform(ks[1], (KX, KY, dv, dv), dtype=jnp.float32)
        R_imag = jax.random.uniform(ks[2], (KX, KY, dv, dv), dtype=jnp.float32)
        W = jax.random.normal(ks[3], (dv, dv), dtype=jnp.float32) * (1.0 / np.sqrt(dv))
        b = jax.random.normal(ks[4], (dv,), dtype=jnp.float32) * 0.05
        return {'x': x, 'R_real': R_real, 'R_imag': R_imag, 'W': W, 'b': b}
    _L3_conv_all = _L3_conv_setup()
    _L3_conv_in = {k: v for k, v in _L3_conv_all.items() if k in ('R_real', 'R_imag', 'W', 'b', )}
    del _L3_conv_all

    return {
        "x": x,
        "L0_conv_W": _L0_conv_in["W"],
        "L0_conv_b": _L0_conv_in["b"],
        "L1_conv_W": _L1_conv_in["W"],
        "L1_conv_b": _L1_conv_in["b"],
        "L2_conv_R_real": _L2_conv_in["R_real"],
        "L2_conv_R_imag": _L2_conv_in["R_imag"],
        "L2_conv_W": _L2_conv_in["W"],
        "L2_conv_b": _L2_conv_in["b"],
        "L3_conv_R_real": _L3_conv_in["R_real"],
        "L3_conv_R_imag": _L3_conv_in["R_imag"],
        "L3_conv_W": _L3_conv_in["W"],
        "L3_conv_b": _L3_conv_in["b"],
    }

def reference(x, L0_conv_W, L0_conv_b, L1_conv_W, L1_conv_b, L2_conv_R_real, L2_conv_R_imag, L2_conv_W, L2_conv_b, L3_conv_R_real, L3_conv_R_imag, L3_conv_W, L3_conv_b):
    import jax
    import jax.numpy as jnp
    def _L0_conv_ref(x, W, b, y):
        import jax, jax.numpy as jnp
        import numpy as np
        MAX_OFFSET = 28
        B, H, Wd, C = x.shape
        mean_feat = jnp.mean(x, axis=(1, 2))
        offsets = mean_feat @ W + b
        offsets = jnp.clip(offsets, 0, MAX_OFFSET).astype(jnp.int32)
        dy, dx = (offsets[:, 0], offsets[:, 1])
        idx = jnp.arange(y)
        src_i = idx[None, :] - dy[:, None]
        src_j = idx[None, :] - dx[:, None]
        vi = (src_i >= 0) & (src_i < H)
        vj = (src_j >= 0) & (src_j < Wd)
        ci = jnp.clip(src_i, 0, H - 1)
        cj = jnp.clip(src_j, 0, Wd - 1)
        bidx = jnp.arange(B)[:, None, None]
        gathered = x[bidx, ci[:, :, None], cj[:, None, :], :]
        mask = (vi[:, :, None] & vj[:, None, :])[..., None]
        return jnp.where(mask, gathered, jnp.zeros((), x.dtype))

    def _L1_conv_ref(x, W, b):
        import jax, jax.numpy as jnp
        from jax import lax
        import numpy as np

        @jax.custom_vjp
        def ste_sign(x):
            return jnp.where(x >= 0, 1.0, -1.0).astype(x.dtype)

        def _ste_fwd(x):
            return (ste_sign(x), x)

        def _ste_bwd(x, g):
            return (g * (jnp.abs(x) <= 1.0).astype(g.dtype),)
        ste_sign.defvjp(_ste_fwd, _ste_bwd)
        xq = ste_sign(x)
        wq = ste_sign(W)
        w_sum = wq.sum(axis=0)
        y = lax.conv_general_dilated(xq, w_sum, window_strides=(1, 1), padding='SAME', dimension_numbers=('NHWC', 'HWIO', 'NHWC'))
        return y + b.sum(axis=0)

    def _L2_conv_ref(x, R_real, R_imag, W, b):
        import jax, jax.numpy as jnp
        import numpy as np
        KX = 32
        KY = 32

        def dct_matrix(N):
            n = jnp.arange(N, dtype=jnp.float32)
            k = n[:, None]
            D = jnp.cos(jnp.pi * (n[None, :] + 0.5) * k / N)
            scale = jnp.where(jnp.arange(N) == 0, jnp.sqrt(1.0 / N), jnp.sqrt(2.0 / N))
            return (D * scale[:, None]).astype(jnp.float32)
        B, nX, nY, dv = x.shape
        R = R_real + 1j * R_imag
        D = dct_matrix(nY)
        v = jnp.moveaxis(x, -1, -3)
        v = jnp.einsum('kn,bcxn->bcxk', D, v)
        v = jnp.fft.rfft(v, axis=-2, norm='ortho')
        vt = v[..., :KX, :KY]
        vt = jnp.einsum('ijab,ejab->eiab', R, vt)
        nXf = nX // 2 + 1
        spec = jnp.zeros((B, dv, nXf, nY), dtype=vt.dtype).at[..., :KX, :KY].set(vt)
        u = jnp.fft.irfft(spec, n=nX, axis=-2, norm='ortho')
        u = jnp.einsum('kn,bcxk->bcxn', D, u)
        v_out = jnp.moveaxis(u, -3, -1)
        w = x @ W.T + b
        return jax.nn.relu(v_out + w)

    def _L3_conv_ref(x, R_real, R_imag, W, b):
        import jax, jax.numpy as jnp
        import numpy as np
        KX = 32
        KY = 32

        def dct_matrix(N):
            n = jnp.arange(N, dtype=jnp.float32)
            k = n[:, None]
            D = jnp.cos(jnp.pi * (n[None, :] + 0.5) * k / N)
            scale = jnp.where(jnp.arange(N) == 0, jnp.sqrt(1.0 / N), jnp.sqrt(2.0 / N))
            return (D * scale[:, None]).astype(jnp.float32)
        B, nX, nY, dv = x.shape
        R = R_real + 1j * R_imag
        D = dct_matrix(nY)
        v = jnp.moveaxis(x, -1, -3)
        v = jnp.einsum('kn,bcxn->bcxk', D, v)
        v = jnp.fft.rfft(v, axis=-2, norm='ortho')
        vt = v[..., :KX, :KY]
        vt = jnp.einsum('ijab,ejab->eiab', R, vt)
        nXf = nX // 2 + 1
        spec = jnp.zeros((B, dv, nXf, nY), dtype=vt.dtype).at[..., :KX, :KY].set(vt)
        u = jnp.fft.irfft(spec, n=nX, axis=-2, norm='ortho')
        u = jnp.einsum('kn,bcxk->bcxn', D, u)
        v_out = jnp.moveaxis(u, -3, -1)
        w = x @ W.T + b
        return jax.nn.relu(v_out + w)

    def _gn(v, G=16, eps=1e-5):
        B_, H_, W_, C_ = v.shape
        g = v.reshape(B_, H_, W_, G, C_ // G)
        m = jnp.mean(g, axis=(1, 2, 4), keepdims=True)
        s = jnp.var(g, axis=(1, 2, 4), keepdims=True)
        return ((g - m) / jnp.sqrt(s + eps)).reshape(v.shape)

    def _ln_c(v, eps=1e-6):
        m = jnp.mean(v, axis=-1, keepdims=True)
        s = jnp.var(v, axis=-1, keepdims=True)
        return (v - m) / jnp.sqrt(s + eps)

    def _ln_t(v, eps=1e-5):
        m = jnp.mean(v, axis=-1, keepdims=True)
        s = jnp.var(v, axis=-1, keepdims=True)
        return (v - m) / jnp.sqrt(s + eps)

    def _to_tokens(v):
        B_, H_, W_, C_ = v.shape
        return v.reshape(B_, H_ * W_, C_)
    def _from_tokens(t, like):
        return t.reshape(like.shape)

    x = x + _L0_conv_ref(_gn(x), L0_conv_W, L0_conv_b, 224)
    x = x + _L1_conv_ref(_gn(x), L1_conv_W, L1_conv_b)
    x = x + _L2_conv_ref(_gn(x), L2_conv_R_real, L2_conv_R_imag, L2_conv_W, L2_conv_b)
    x = x + _L3_conv_ref(_gn(x), L3_conv_R_real, L3_conv_R_imag, L3_conv_W, L3_conv_b)
    return x


_drawn_inputs = setup_inputs


def setup_inputs(seed=0):
    import zlib

    import numpy as np

    out = dict(_drawn_inputs(seed))
    spreads = {'L1_conv_b': (0.0, 0.8)}
    factors = {'L2_conv_R_real': 7.011,
     'L2_conv_R_imag': 7.058,
     'L2_conv_W': 3.229,
     'L2_conv_b': 64.0,
     'L3_conv_R_real': 7.056,
     'L3_conv_R_imag': 7.104,
     'L3_conv_W': 3.208,
     'L3_conv_b': 64.0}
    for name, (base, spread) in spreads.items():
        noise = np.random.default_rng([zlib.crc32(name.encode()), seed]).standard_normal(out[name].shape)
        drawn = base * np.exp(spread * noise) if base else spread * noise
        out[name] = jnp.asarray(drawn.astype(out[name].dtype))
    for name, factor in factors.items():
        out[name] = (out[name] * factor).astype(out[name].dtype)
    return out
```

```python
import concourse.bass as bass
from concourse import mybir
from contextlib import ExitStack
import numpy as np

f32 = mybir.dt.float32
bf16 = mybir.dt.bfloat16
i32 = mybir.dt.int32
ALU = mybir.AluOpType
ACT = mybir.ActivationFunctionType
AX = mybir.AxisListType

SIZE = 224
C = 32
P = 128
HR = SIZE // 2
QG = P // C
NBLK = SIZE // QG
PAIRS = HR // 16
UNITS = 4 * PAIRS
TILES = 2 * PAIRS
BLKU = 16 // QG
COLS = BLKU * HR
BANK = 512
MODES = 32
KP = 2 * MODES
MAXOFF = 28
EPS = 1e-5
NPIX = SIZE * SIZE // QG
RP = SIZE + 4
CMB = MAXOFF // QG


def constants():
    r = np.arange(SIZE, dtype=np.float64)
    n = np.arange(MODES, dtype=np.float64)
    root = np.sqrt(1.0 / SIZE)
    ang = 2 * np.pi * np.outer(n, r) / SIZE
    fwd = np.stack([np.cos(ang), -np.sin(ang)]) * root
    fwd = fwd.reshape(2, 2, 16, SIZE).transpose(1, 0, 2, 3)
    fwd = fwd.reshape(KP, 2, HR).transpose(2, 1, 0)
    wgt = np.where(n == 0, 1.0, 2.0)[:, None]
    inv = np.stack([np.cos(ang), -np.sin(ang)]) * root * wgt
    inv = inv.reshape(2, 2, 8, 2, SIZE).transpose(3, 0, 1, 2, 4).reshape(KP, 2, HR)
    invz = np.zeros((P, 2, 2, HR))
    invz[0:KP, 0], invz[KP:P, 1] = inv, inv
    dct = np.cos(np.pi * (r[None, :] + 0.5) * n[:, None] / SIZE)
    dct *= np.where(n == 0, root, np.sqrt(2.0 / SIZE))[:, None]
    dctf = dct.reshape(MODES, 2, HR).transpose(2, 1, 0)
    p = np.arange(P)
    ch = p % C
    pair = (ch[:, None] // 2 == ch[None, :] // 2) / (2.0 * QG)
    same = (ch[:, None] == ch[None, :]) / float(QG)
    cols = QG * np.arange(CMB)[None, :] + (p // C)[:, None]
    out = {
        "k_fwd": fwd, "k_inv": invz, "k_dctf": dctf, "k_dcti": np.tile(dct, (4, 1)),
        "k_ident": np.eye(P), "k_pair": pair, "k_pairn": pair / NPIX, "k_same": same,
        "k_rows": np.tile(np.arange(MAXOFF), (P, 1)), "k_cols": cols,
    }
    return {k: np.ascontiguousarray(v, dtype=np.float32) for k, v in out.items()}


class Semaphores:

    def __init__(self, nc):
        self.nc, self.made = nc, []

    def new(self, name):
        self.made.append(self.nc.alloc_semaphore(name))
        return self.made[-1]

    def __enter__(self):
        return self

    def __exit__(self, *failed):
        if failed[0] is None:
            self.nc.clear_and_free_semaphores(self.made)
            self.nc.all_engine_barrier()


def load_constants(nc, sb, tag, names):
    out = {}
    with Semaphores(nc) as sems, nc.Block() as block:
        const_loaded = sems.new(tag + "const_loaded")
        for key, (src, shape) in names.items():
            out[key] = sb(tag + key, shape, f32)

        @block.sync
        def _(sp):
            for key, (src, shape) in names.items():
                sp.dma_start(out[key][:], src).then_inc(const_loaded, 16)
            sp.wait_ge(const_loaded, 16 * len(names))
    return out


def blk_of(v):
    u, side = divmod(v, 2)
    return side * (NBLK // 2) + BLKU * (u // 2)


def shift_conv_forward(nc, NB, x, w1, b1, w0, b0, con, statm, xpad, x2s, spec):
    ctx = ExitStack()
    with Semaphores(nc) as sems, ctx:
        def sb(name, shape, dt=f32):
            return ctx.enter_context(nc.sbuf_tensor("A_" + name, shape, dt))

        def sem(name):
            return sems.new("A_" + name)

        RING = 4
        image = [sb(f"image{i}", [P, NBLK, SIZE]) for i in range(2)]
        signa = sb("signa", [P, NBLK * RP], bf16)
        signb = sb("signb", [P, NBLK * RP], bf16)
        tin = [sb(f"tin{i}", [HR, 2, BANK]) for i in range(RING)]
        OUTS = 4
        tout = [sb(f"tout{i}", [HR, 2, BANK]) for i in range(2)]
        rowspec = sb("rowspec", [P, PAIRS, BANK])
        shared = sb("shared", [P, 2, 2 * BANK])
        shifted = [shared[:, i // 2, (i % 2) * BANK:(i % 2) * BANK + COLS].rearrange("p (j r) -> p j r", r=HR)
                   for i in range(4)]
        tout += [shared[0:HR, i, :].rearrange("p (s m) -> p s m", s=2) for i in range(2)]
        uses = [len(range(i, TILES, OUTS)) for i in range(OUTS)]
        junk = [sb(f"junk{i}", [P, BLKU, SIZE], bf16) for i in range(2)]
        stat = sb("stat", [P, UNITS, 6])
        addsum = sb("addsum", [P, UNITS])
        convsum = sb("convsum", [P, UNITS])
        convsq = sb("convsq", [P, UNITS // 2])
        mv = sb("mv", [P, 2])
        carrier = sb("carrier", [P, 1])
        sm = sb("sm", [P, 32])
        lin = [sb(f"lin{i}", [P, 2]) for i in range(2)]
        rmask = [sb(f"rmask{i}", [P, MAXOFF]) for i in range(2)]
        cmask = [sb(f"cmask{i}", [P, CMB]) for i in range(2)]
        offi = sb("offi", [P, 2], i32)
        wsc = sb("wsc", [C, 2])
        early = image[1][:, :, :].rearrange("p j r -> p (j r)")
        wraw = early[:, 0:36 * C].rearrange("p (m t c) -> p m t c", m=4, c=C)
        wsum = early[:, 36 * C:45 * C].rearrange("p (t c) -> p t c", c=C)
        zrow = early[0:29, 48 * C:48 * C + BANK]
        wtap = sb("wtap", [P, QG, C])
        cwa = sb("cwa", [P, 3, 2 * C], bf16)
        cwb = sb("cwb", [P, 3, 2 * C], bf16)
        braw = sb("braw", [4, QG, C])
        w0s = sb("w0s", [C, 2])
        b0s = sb("b0s", [P, 2])
        ones = sb("ones", [P, P])
        mones = sb("mones", [P, 1])
        bias = sb("bias", [P, 1])
        epst = sb("epst", [P, 1])
        m1 = sb("m1", [P, 1])
        nk = sb("nk", [P, 1])

        def three(t):
            return t[:, :].rearrange("p (j r) -> p j r", r=RP)
        sa, sbb = three(signa), three(signb)
        colspec = signa[0:HR, 0:2 * P * C].bitcast(f32).rearrange("p (k c) -> p k c", c=C)

        tps = [ctx.enter_context(nc.psum_tensor(f"A_tps{i}", [P, BANK], f32)) for i in range(2)]
        cps = [ctx.enter_context(nc.psum_tensor(f"A_cps{i}", [P, BANK], f32)) for i in range(2)]
        xps = [ctx.enter_context(nc.psum_tensor(f"A_xps{i}", [P, BANK], f32)) for i in range(2)]
        vps = ctx.enter_context(nc.psum_tensor("A_vps", [P, BANK], f32))
        mps = ctx.enter_context(nc.psum_tensor("A_mps", [P, BANK], f32))

        N_TURN = 2 * UNITS + 8
        in_full = [sem(f"in_full{i}") for i in range(RING)]
        pad_done = sem("pad_done")
        off_ready = sem("off_ready")
        off_seen = sem("off_seen")
        off_taken = sem("off_taken")
        turn_full = sem("turn_full")
        turn_copied = sem("turn_copied")
        shift_added = sem("shift_added")
        conv_full = sem("conv_full")
        conv_added = sem("conv_added")
        x_full = sem("x_full")
        tout_full = sem("tout_full")
        tout_read = sem("tout_read")
        rowspec_full = sem("rowspec_full")
        spec_full = sem("spec_full")
        stored = [sem(f"stored{i}") for i in range(OUTS)]
        spec_stored = sem("spec_stored")
        spec_sb = sem("spec_sb")
        sign_full = sem("sign_full")
        mean_in = sem("mean_in")
        mean_out = sem("mean_out")
        var_in = sem("var_in")
        var_out = sem("var_out")
        nk_ready = sem("nk_ready")
        sq_done = sem("sq_done")
        dve_step = sem("dve_step")
        act_step = sem("act_step")
        wload = sem("wload")
        setup = sem("setup")
        lin_ready = sem("lin_ready")
        specout = sb("specout", [P, BANK])
        MEANS = 4
        block = ctx.enter_context(nc.Block())

        x_pix = x.rearrange("b r q c -> (b r q) c")
        pad_pix = xpad.rearrange("r q c -> (r q) c")

        def tile_src(flat, u):
            rows = flat.rearrange("(r s q) c -> r s (q c)", s=2, q=HR)
            p = u // 2
            return rows[:, :, 16 * p * C:16 * (p + 1) * C]

        @block.sync
        def _(sp):
            sp.sem_inc(spec_stored, 16)
            sp.wait_ge(setup, 1)
            for g in range(SIZE * C // BANK):
                sp.dma_start(xpad[0:29].rearrange("r q c -> r (q c)")[:, g * BANK:(g + 1) * BANK],
                             zrow).then_inc(pad_done, 16)
            sp.dma_start(xpad[29:29 + HR].rearrange("r q c -> r (q c)"),
                         x[0, 0:HR].rearrange("r q c -> r (q c)")).then_inc(pad_done, 16)
            sp.wait_ge(pad_done, 16 * (SIZE * C // BANK + 1))

            def load(flat, lane, read):
                if read is not None:
                    sp.wait_ge(turn_full, read)
                sp.dma_start(tin[lane % RING][:], flat).then_inc(in_full[lane % RING], 16)

            def reads(first, before, u):
                if u >= RING:
                    return first + 2 * (u - RING) + 2
                return None if before is None else before + 2 * (TILES - RING + u) + 2

            def plain(b, first, before):
                for u in range(TILES):
                    start = b * (SIZE * SIZE) + (u % 2) * (HR * SIZE)
                    load(tile_src(x_pix[bass.ds(start, HR * SIZE), :], u), u, reads(first, before, u))

            def moved(b, first, before, image0):
                sp.wait_ge(off_ready, b + 1)
                sp.sem_inc(off_seen, 1)
                dy = sp.value_load(offi[0:1, 0:1], min_val=0, max_val=MAXOFF)
                dx = sp.value_load(offi[0:1, 1:2], min_val=0, max_val=MAXOFF)
                back = dy * SIZE + dx
                sp.sem_inc(off_taken, 1)
                for u in range(TILES):
                    half = u % 2
                    if image0 and half == 0:
                        flat = pad_pix[bass.ds(29 * SIZE - back, HR * SIZE), :]
                    else:
                        flat = x_pix[bass.ds(b * (SIZE * SIZE) + half * (HR * SIZE) - back, HR * SIZE), :]
                    load(tile_src(flat, u), TILES + u, reads(first, before, u))

            def store_spec(b):
                sp.wait_ge(spec_sb, b + 2)
                sp.dma_start(spec[bass.ds(b, 1)].rearrange("o p m -> (o p) m"), specout[:]).then_inc(spec_stored, 16)

            plain(0, 0, None)
            moved(0, UNITS, 0, True)
            plain(1, 2 * UNITS, UNITS)
            with sp.Fori(1, NB - 1) as b:
                moved(b, UNITS + b * N_TURN, b * N_TURN - 8, False)
                store_spec(b - 1)
                plain(b + 1, 2 * UNITS + b * N_TURN, UNITS + b * N_TURN)
            moved(NB - 1, UNITS + (NB - 1) * N_TURN, (NB - 1) * N_TURN - 8, False)
            store_spec(NB - 2)
            store_spec(NB - 1)
            sp.wait_ge(spec_stored, 16 * NB + 16)

        def turn(pe, src, v, seq):
            if not isinstance(seq, int) or seq >= 2:
                pe.wait_ge(turn_copied, seq - 1)
            dst = tps[v % 2]
            for j in range(BLKU):
                last = nc.tensor.transpose(dst[:, j * HR:(j + 1) * HR], src[:, v % 2, j * P:(j + 1) * P],
                                           con["k_ident"][0:HR, 0:HR])
            return last.then_inc(turn_full, 1)

        @block.tensor
        def _(pe):
            pe.sem_inc(tout_read, 1)
            pe.wait_ge(setup, 2)
            nc.tensor.matmul(mps[:, 0:1], wtap[0:C, :, :], mones[0:C, :], start=True, stop=False)
            nc.tensor.matmul(mps[:, 0:1], braw[:, :, :], ones[0:4, 0:1], start=False, stop=True).then_inc(mean_out, 1)

            def average(b, k, mats, seq_extra=0):
                pe.wait_ge(mean_in, k)
                for out, lhs, rhs in mats:
                    last = nc.tensor.matmul(out, lhs, rhs, start=True, stop=True)
                last.then_inc(mean_out, 1)

            def statistics(k, i):
                if i == 1:
                    average(None, k + 1, [(mps[:, 2:3], con["k_pair"][:], mv[:, 0:1]), (mps[:, 3:4], con["k_same"][:], mv[:, 0:1])])
                elif i == 2:
                    average(None, k + 2, [(mps[:, 4:5], con["k_pair"][:], sm[:, 2:3])])
                else:
                    average(None, k + 3, [(mps[:, 6:8], ones[0:C, :], wsc[:])])

            for u in range(TILES):
                slot = u % RING
                pe.wait_ge(in_full[slot], (u // RING + 1) * 16)
                for side in range(2):
                    turn(pe, tin[slot], 2 * u + side, 2 * u + side)
            for i in (1, 2, 3):
                statistics(0, i)

            def body(b, par, last_image):
                img = image[par]
                seq0 = UNITS + b * N_TURN
                for u in range(TILES):
                    slot = (TILES + u) % RING
                    pe.wait_ge(in_full[slot], (b * 7 + (TILES + u) // RING + 1) * 16)
                    for side in range(2):
                        turn(pe, tin[slot], 2 * u + side, seq0 + 2 * u + side)
                average(b, b * MEANS + 3 + 1, [(mps[:, 8:9], con["k_pairn"][:], sm[:, 8:9])])
                if not last_image:
                    for u in range(TILES):
                        slot = u % RING
                        pe.wait_ge(in_full[slot], ((b + 1) * 7 + u // RING + 1) * 16)
                        for side in range(2):
                            turn(pe, tin[slot], 2 * u + side, seq0 + UNITS + 2 * u + side)
                turned = seq0 + (UNITS if last_image else 2 * UNITS)

                pe.wait_ge(sign_full, b + 1)
                conv_no = 0
                for step in range(PAIRS + 2):
                    if step < PAIRS:
                        for k in range(4):
                            j0 = (k // 2) * (NBLK // 2) + BLKU * step + 2 * (k % 2)
                            pe.wait_ge(conv_added, b * UNITS + conv_no + 1)
                            dst = cps[conv_no % 2]
                            for tap in range(3):
                                for g, (src, wts) in enumerate(((sa, cwa), (sbb, cwb))):
                                    last = nc.tensor.matmul(
                                        dst[64 * g:64 * g + 64, 0:COLS], wts[:, tap, :],
                                        src[:, j0:j0 + 2, 1 + tap:1 + tap + SIZE],
                                        start=(tap == 0), stop=(tap == 2), skip_group_check=True)
                            last.then_inc(conv_full, 1)
                            conv_no += 1
                    if step >= 2:
                        p = step - 2
                        pe.wait_ge(rowspec_full, b * PAIRS + p + 1)
                        if p == 0:
                            pe.wait_ge(spec_sb, b + 1)
                        for half in range(2):
                            u = 2 * p + half
                            pe.wait_ge(tout_full, b * UNITS + 2 * u + 2 + 2)
                            for side in range(2):
                                last = nc.tensor.matmul(vps[64 * side:64 * side + 64, :], con["k_fwd"][:, half, :],
                                                        tout[u % OUTS][:, side, :], start=(half == 0), stop=(half == 1),
                                                        skip_group_check=True)
                            last.then_inc(tout_read, 1)
                    if step == PAIRS and not last_image:
                        statistics(b * MEANS + 4, 2)
                    if 1 <= step <= PAIRS:
                        p = step - 1
                        pe.wait_ge(conv_added, b * UNITS + 4 * (p + 1) + 2)
                        for v in range(4 * p, 4 * p + 4):
                            pe.wait_ge(tout_full, b * UNITS + v + 1)
                            half = (v // 2) % 2
                            for j in range(BLKU):
                                last = nc.tensor.transpose(
                                    xps[v % 2][0:HR, j * P:(j + 1) * P],
                                    img[:, blk_of(v) + j, half * HR:(half + 1) * HR], con["k_ident"][:])
                            last.then_inc(x_full, 1)
                    if PAIRS - 1 <= step <= PAIRS and not last_image:
                        statistics(b * MEANS + 4, 1 if step == PAIRS - 1 else 3)
                pe.wait_ge(rowspec_full, (b + 1) * PAIRS + 1)
                rs = rowspec[:, :, :].rearrange("p n (q c) -> p (n q) c", c=C)
                for k in range(8):
                    pe.wait_ge(turn_copied, turned + k - 1)
                    for j in range(4):
                        last = nc.tensor.transpose(tps[k % 2][0:HR, j * P:(j + 1) * P], rs[:, :, 4 * k + j], con["k_ident"][:])
                    last.then_inc(turn_full, 1)
                pe.wait_ge(turn_copied, turned + 8)
                for side in range(2):
                    for g in range(4):
                        last = nc.tensor.matmul(
                            vps[32 * g:32 * g + 32, :], con["k_dctf"][:, side, :],
                            colspec[:, side * KP + 16 * g:side * KP + 16 * g + 16, :].rearrange("p k c -> p (k c)"),
                            start=(side == 0), stop=(side == 1), skip_group_check=True)
                last.then_inc(spec_full, 1)

            with pe.Fori(0, NB // 2 - 1) as i:
                body(2 * i, 0, False)
                body(2 * i + 1, 1, False)
            body(NB - 2, 0, False)
            body(NB - 1, 1, True)

        @block.scalar
        def _(act):
            act.sem_inc(tout_full, 2)
            act.sem_inc(sq_done, 2)
            act.sem_inc(rowspec_full, 1)
            for i in range(OUTS):
                act.sem_inc(stored[i], 16)

            def root(k):
                act.wait_ge(var_in, k)
                nc.scalar.activation(sm[:, 4:5], sm[:, 3:4], ACT.Sqrt, bias=epst[:]).then_inc(var_out, 1)

            for v in range(UNITS):
                act.wait_ge(turn_full, v + 1)
                half = (v // 2) % 2
                nc.scalar.activation(image[0][:, blk_of(v):blk_of(v) + BLKU, half * HR:(half + 1) * HR],
                                     tps[v % 2][:, 0:COLS].rearrange("p (j r) -> p j r", r=HR),
                                     ACT.Copy).then_inc(turn_copied, 1)
            root(1)

            def body(b, par, last_image):
                img = image[par]
                seq0 = UNITS + b * N_TURN
                act.wait_ge(lin_ready, b + 1)
                act.wait_ge(tout_read, b * TILES + 1)
                for i in range(2, OUTS):
                    act.wait_ge(stored[i], b * uses[i] * 16 + 16)
                for v in range(UNITS):
                    act.wait_ge(turn_full, seq0 + v + 1)
                    act.wait_ge(shift_added, b * UNITS + v + 1)
                    nc.scalar.activation(shifted[v % 4][:, :, :], tps[v % 2][:, 0:COLS].rearrange("p (j r) -> p j r", r=HR),
                                         ACT.Identity, bias=lin[par][:, 1:2], scale=lin[par][:, 0:1]).then_inc(turn_copied, 1)
                if not last_image:
                    for v in range(UNITS):
                        act.wait_ge(turn_full, seq0 + UNITS + v + 1)
                        half = (v // 2) % 2
                        nc.scalar.activation(image[1 - par][:, blk_of(v):blk_of(v) + BLKU, half * HR:(half + 1) * HR],
                                             tps[v % 2][:, 0:COLS].rearrange("p (j r) -> p j r", r=HR),
                                             ACT.Copy).then_inc(turn_copied, 1)
                turned = seq0 + (UNITS if last_image else 2 * UNITS)
                act.wait_ge(nk_ready, b + 1)

                def store(u):
                    act.wait_ge(tout_full, b * UNITS + 2 * u + 2 + 2)
                    act.dma_start(x2s[bass.ds(b, 1), u].rearrange("o p m -> (o p) m"),
                                  tout[u % OUTS][:, :, :].rearrange("p s m -> p (s m)")).then_inc(stored[u % OUTS], 16)

                for p in range(PAIRS):
                    for v in range(4 * p, 4 * p + 4):
                        u = v // 2
                        act.wait_ge(x_full, b * UNITS + v + 1)
                        if v % 2 == 0:
                            slot = u % OUTS
                            act.wait_ge(tout_read, b * TILES + (u - OUTS + 1 if u >= OUTS else 0) + 1)
                            act.wait_ge(stored[slot], (b * uses[slot] + u // OUTS) * 16 + 16)
                        nc.scalar.activation(tout[u % OUTS][:, v % 2, :], xps[v % 2][0:HR, :], ACT.Copy).then_inc(tout_full, 1)
                        if v % 2 == 0 and u >= 1:
                            store(u - 1)
                    if p == PAIRS - 1 and not last_image:
                        root(b + 2)
                    for side in range(2):
                        j0 = side * (NBLK // 2) + BLKU * p
                        act.wait_ge(sq_done, b * (UNITS // 2) + 2 * p + side + 1)
                        nc.scalar.activation(junk[side][:], img[:, j0:j0 + BLKU, :],
                                             ACT.Square, bias=nk[:], accum_out=convsq[:, 2 * p + side:2 * p + side + 1]).then_inc(sq_done, 1)
                    if p >= 1:
                        act.wait_ge(tout_read, b * TILES + 2 * p + 1)
                        nc.scalar.activation(rowspec[:, p - 1, :], vps[:, :], ACT.Copy).then_inc(rowspec_full, 1)
                store(TILES - 1)
                act.wait_ge(tout_read, (b + 1) * TILES + 1)
                nc.scalar.activation(rowspec[:, PAIRS - 1, :], vps[:, :], ACT.Copy).then_inc(rowspec_full, 1)
                for k in range(8):
                    act.wait_ge(turn_full, turned + k + 1)
                    nc.scalar.activation(colspec[:, :, 4 * k:4 * k + 4].rearrange("p k c -> p c k"),
                                         tps[k % 2][0:HR, :].rearrange("p (c k) -> p c k", k=P), ACT.Copy).then_inc(turn_copied, 1)

            with act.Fori(0, NB // 2 - 1) as i:
                body(2 * i, 0, False)
                body(2 * i + 1, 1, False)
            body(NB - 2, 0, False)
            body(NB - 1, 1, True)
            for i in range(OUTS):
                act.wait_ge(stored[i], NB * uses[i] * 16 + 16)

        @block.vector
        def _(dve):
            at = {"base": 0, "n": 0}

            def link(ins):
                at["n"] += 1
                ins.then_inc(dve_step, 1)
                dve.wait_ge(dve_step, at["base"] + at["n"])

            dve.sem_inc(shift_added, 4)
            dve.sem_inc(conv_added, 2)
            dve.sem_inc(spec_sb, 1)
            nc.vector.memset(zrow, 0.0).then_inc(setup, 1)
            dve.wait_ge(wload, 16 * 7)
            link(nc.vector.tensor_scalar(wraw, wraw, 0.0, None, ALU.is_ge))
            link(nc.vector.tensor_tensor(wraw[:, 0:2], wraw[:, 0:2], wraw[:, 2:4], ALU.add))
            link(nc.vector.tensor_tensor(wsum, wraw[:, 0], wraw[:, 1], ALU.add))
            link(nc.vector.tensor_scalar(wsum, wsum, 2.0, -4.0, ALU.mult, ALU.add))
            link(nc.vector.tensor_reduce(wtap[:, 0, :], wsum[:, :, :].rearrange("p t c -> p c t"), AX.X, ALU.add))
            for g in range(1, QG):
                nc.vector.tensor_copy(wtap[:, g, :], wtap[:, 0, :])
            nc.vector.memset(ones[:], 1.0)
            nc.vector.memset(mones[:], -1.0)
            nc.vector.memset(epst[:], EPS)
            nc.vector.memset(cwa[:], 0.0)
            nc.vector.memset(cwb[:], 0.0)
            nc.vector.memset(signa[:], 1.0)
            link(nc.vector.memset(signb[:], 1.0))
            w4 = wsum[:, :, :].rearrange("p (h w) c -> p h w c", w=3)
            for wts, outs in ((cwa, ((0, (3, 0, 1)), (1, (0, 1, 2)))), (cwb, ((0, (1, 2, 3)), (1, (2, 3, 0))))):
                for o, groups in outs:
                    for kw, g in enumerate(groups):
                        last = nc.vector.tensor_copy(wts[32 * g:32 * g + 32, :, 32 * o:32 * o + 32],
                                                     w4[32 * g:32 * g + 32, :, kw, :])
            last.then_inc(setup, 1)
            dve.wait_ge(mean_out, 1)
            link(nc.vector.tensor_copy(bias[:], mps[:, 0:1]))
            SETUP = at["n"]

            def statistics(b, k, par):
                n0 = at["n"]
                nc.vector.memset(carrier[:], 0.0)
                link(nc.vector.bn_aggr(mv[:], stat[:, :, :].rearrange("p n s -> p (n s)")))
                dve.sem_inc(mean_in, 1)
                dve.wait_ge(mean_out, 1 + k + 1)
                link(nc.vector.tensor_copy(sm[:, 0:2], mps[:, 2:4]))
                link(nc.vector.tensor_tensor(sm[:, 10:11], mv[:, 0:1], sm[:, 0:1], ALU.subtract))
                link(nc.vector.scalar_tensor_tensor(out=sm[:, 2:3], in0=sm[:, 10:11], scalar=sm[:, 10:11], in1=mv[:, 1:2],
                                                    op0=ALU.mult, op1=ALU.add))
                dve.sem_inc(mean_in, 1)
                dve.wait_ge(mean_out, 1 + k + 2)
                link(nc.vector.tensor_copy(sm[:, 3:4], mps[:, 4:5]))
                dve.sem_inc(var_in, 1)
                dve.wait_ge(var_out, b + 1)
                link(nc.vector.reciprocal(lin[par][:, 0:1], sm[:, 4:5]))
                link(nc.vector.scalar_tensor_tensor(out=lin[par][:, 1:2], in0=sm[:, 0:1], scalar=-1.0,
                                                    in1=lin[par][:, 0:1], op0=ALU.mult, op1=ALU.mult))
                dve.sem_inc(lin_ready, 1)
                link(nc.vector.scalar_tensor_tensor(out=sm[:, 11:12], in0=sm[:, 1:2], scalar=sm[:, 0:1],
                                                    in1=lin[par][:, 0:1], op0=ALU.subtract, op1=ALU.mult))
                link(nc.vector.tensor_scalar(wsc[:], w0s[:], sm[0:C, 11:12], None, ALU.mult))
                dve.sem_inc(mean_in, 1)
                dve.wait_ge(mean_out, 1 + k + 3)
                link(nc.vector.tensor_tensor(sm[:, 12:14], mps[:, 6:8], b0s[:], ALU.add))
                link(nc.vector.tensor_scalar(sm[:, 12:14], sm[:, 12:14], 0.0, float(MAXOFF), ALU.max, ALU.min))
                if not (isinstance(b, int) and b == 0):
                    dve.wait_ge(off_taken, b)
                link(nc.vector.tensor_copy(offi[:], sm[:, 12:14]))
                link(nc.vector.tensor_copy(sm[:, 14:16], offi[:]))
                link(nc.vector.tensor_tensor(sm[:, 16:18], sm[:, 14:16], sm[:, 12:14], ALU.is_gt))
                link(nc.vector.tensor_tensor(sm[:, 18:20], sm[:, 14:16], sm[:, 16:18], ALU.subtract))
                link(nc.vector.tensor_copy(offi[:], sm[:, 18:20]))
                dve.sem_inc(off_ready, 1)
                link(nc.vector.tensor_scalar(rmask[par][:], con["k_rows"][:], sm[:, 18:19], None, ALU.is_ge))
                link(nc.vector.tensor_scalar(cmask[par][:], con["k_cols"][:], sm[:, 19:20], None, ALU.is_ge))
                return at["n"] - n0

            for v in range(UNITS):
                half = (v // 2) % 2
                dve.wait_ge(turn_copied, v + 1)
                last = nc.vector.bn_stats(stat[:, v, :], image[0][:, blk_of(v):blk_of(v) + BLKU, half * HR:(half + 1) * HR])
            link(last)
            statistics(0, 0, 0)
            SETUP = at["n"]

            def body(b, par, last_image, per):
                img = image[par]
                seq0 = UNITS + b * N_TURN
                at["base"] = SETUP + b * per
                at["n"] = 0
                for v in range(UNITS):
                    u = v // 2
                    t = shifted[v % 4]
                    dve.wait_ge(turn_copied, seq0 + v + 1)
                    if u % 2 == 0:
                        link(nc.vector.tensor_tensor(t[:, :, 0:MAXOFF], t[:, :, 0:MAXOFF],
                                                     rmask[par][:, None, :].to_broadcast([P, BLKU, MAXOFF]), ALU.mult))
                    nb = min(BLKU, CMB - blk_of(v)) if v % 2 == 0 else 0
                    if nb > 0:
                        j0 = blk_of(v)
                        link(nc.vector.tensor_tensor(t[:, 0:nb, :], t[:, 0:nb, :],
                                                     cmask[par][:, j0:j0 + nb, None].to_broadcast([P, nb, HR]), ALU.mult))
                    half = u % 2
                    dst = img[:, blk_of(v):blk_of(v) + BLKU, half * HR:(half + 1) * HR]
                    nc.vector.scalar_tensor_tensor(out=dst, in0=t[:, :, :], scalar=1.0, in1=dst, op0=ALU.mult, op1=ALU.add,
                                                   accum_out=addsum[:, v:v + 1]).then_inc(shift_added, 1)
                dve.wait_ge(shift_added, 4 + (b + 1) * UNITS)
                link(nc.vector.tensor_reduce(sm[:, 8:9], addsum[:], AX.X, ALU.add))
                dve.sem_inc(mean_in, 1)
                dve.wait_ge(mean_out, 1 + b * MEANS + 4)
                link(nc.vector.tensor_copy(m1[:], mps[:, 8:9]))
                link(nc.vector.scalar_tensor_tensor(out=nk[:], in0=m1[:], scalar=-1.0, in1=bias[:], op0=ALU.mult, op1=ALU.subtract))
                dve.sem_inc(nk_ready, 1)
                for k in range(4):
                    last = nc.vector.tensor_scalar(sa[:, 14 * k:14 * k + 14, 2:2 + SIZE], img[:, 14 * k:14 * k + 14, :],
                                                   m1[:], 2.0, ALU.is_ge, ALU.mult)
                nc.vector.memset(sa[:, :, 1:2], 1.0)
                link(nc.vector.memset(sa[:, :, 2 + SIZE:3 + SIZE], 1.0))
                link(nc.vector.tensor_copy(sbb[:, :, 2:2 + SIZE], sa[:, :, 2:2 + SIZE]))
                nc.vector.tensor_copy(sbb[0:32, 0:NBLK - 1, 2:2 + SIZE], sa[0:32, 1:NBLK, 2:2 + SIZE])
                nc.vector.memset(sbb[0:32, NBLK - 1, 2:2 + SIZE], 1.0)
                nc.vector.tensor_copy(sa[96:128, 1:NBLK, 2:2 + SIZE], sbb[96:128, 0:NBLK - 1, 2:2 + SIZE])
                nc.vector.memset(sa[96:128, 0, 2:2 + SIZE], 1.0).then_inc(sign_full, 1)
                conv_no = 0
                for p in range(PAIRS):
                    for k in range(4):
                        j0 = (k // 2) * (NBLK // 2) + BLKU * p + 2 * (k % 2)
                        dve.wait_ge(conv_full, b * UNITS + conv_no + 1)
                        dst = img[:, j0:j0 + 2, :]
                        ins = nc.vector.scalar_tensor_tensor(
                            out=dst, in0=cps[conv_no % 2][:, 0:COLS].rearrange("p (j r) -> p j r", r=SIZE), scalar=bias[:],
                            in1=dst, op0=ALU.add, op1=ALU.add, accum_out=convsum[:, conv_no:conv_no + 1])
                        ins.then_inc(conv_added, 1)
                        if not last_image:
                            v = conv_no
                            half = (v // 2) % 2
                            dve.wait_ge(turn_copied, seq0 + UNITS + v + 1)
                            last = nc.vector.bn_stats(stat[:, v, :], image[1 - par][:, blk_of(v):blk_of(v) + BLKU,
                                                                                    half * HR:(half + 1) * HR])
                        conv_no += 1
                if not last_image:
                    link(last)
                    statistics(b + 1, b * MEANS + 4, 1 - par)
                dve.wait_ge(conv_added, (b + 1) * UNITS + 2)
                dve.wait_ge(sq_done, (b + 1) * (UNITS // 2) + 2)
                link(nc.vector.tensor_reduce(sm[:, 20:21], convsum[:], AX.X, ALU.add))
                link(nc.vector.tensor_reduce(sm[:, 21:22], convsq[:], AX.X, ALU.add))
                mean = statm[:, bass.ds(b, 1), 0:1].rearrange("p o s -> p (o s)")
                var = statm[:, bass.ds(b, 1), 1:2].rearrange("p o s -> p (o s)")
                link(nc.vector.tensor_scalar(sm[:, 22:23], sm[:, 20:21], 1.0 / NPIX, None, ALU.mult))
                nc.vector.tensor_copy(mean, sm[:, 22:23])
                link(nc.vector.tensor_scalar(sm[:, 23:24], sm[:, 22:23], nk[:], None, ALU.add))
                link(nc.vector.tensor_tensor(sm[:, 24:25], sm[:, 23:24], sm[:, 23:24], ALU.mult))
                link(nc.vector.scalar_tensor_tensor(out=sm[:, 25:26], in0=sm[:, 21:22], scalar=1.0 / NPIX, in1=sm[:, 24:25],
                                                    op0=ALU.mult, op1=ALU.subtract))
                nc.vector.tensor_copy(var, sm[:, 25:26])
                dve.wait_ge(spec_full, b + 1)
                dve.wait_ge(spec_stored, b * 16 + 16)
                nc.vector.transpose(specout[:], vps[:, :]).then_inc(spec_sb, 1)
                assert last_image or at["n"] == per, at["n"]

            PER = 48
            with dve.Fori(0, NB // 2 - 1) as i:
                body(2 * i, 0, False, PER)
                body(2 * i + 1, 1, False, PER)
            body(NB - 2, 0, False, PER)
            body(NB - 1, 1, True, PER)

        @block.gpsimd
        def _(pool):
            for g in range(QG):
                pool.dma_start(wraw[32 * g:32 * g + 32, :, :, :],
                               w1.rearrange("m h w i o -> i m (h w) o")).then_inc(wload, 16)
            pool.dma_start(braw[:, :, :], b1[:, None, :].to_broadcast([4, QG, C])).then_inc(wload, 16)
            pool.dma_start(w0s[:], w0).then_inc(wload, 16)
            pool.dma_start(b0s[:], b0[None, :].to_broadcast([P, 2])).then_inc(wload, 16)


def mix_modes(nc, NB, rre, rim, wt, bb, con, statm, gscale, spec, mixed, tag):
    ctx = ExitStack()
    with Semaphores(nc) as sems, ctx:
        def sb(name, shape, dt=f32):
            return ctx.enter_context(nc.sbuf_tensor("M" + tag + name, shape, dt))

        def sem(name):
            return sems.new("M" + tag + name)

        CH = 4
        CHUNKS = 16 // CH
        CM = CH * MODES
        raw = sb("raw", [P, NB, BANK])
        moving = sb("moving", [P, BANK, 2 * NB])
        wmode = [sb(f"wmode{i}", [P, 2 * C, CM]) for i in range(2)]
        mixd = sb("mixd", [P, NB, BANK])
        work = sb("work", [P, 6, NB])
        wts = sb("wts", [C, C])
        bcol = sb("bcol", [C, 1])
        wb = sb("wb", [C, NB])
        epst = sb("epst", [P, 1])
        ps = [ctx.enter_context(nc.psum_tensor(f"M{tag}ps{i}", [P, BANK], f32)) for i in range(4)]
        sps = ctx.enter_context(nc.psum_tensor(f"M{tag}sps", [P, BANK], f32))
        small_in = sem("small_in")
        w_full = [sem(f"w_full{i}") for i in range(2)]
        w_neg = sem("w_neg")
        used = sem("used")
        zeroed = sem("zeroed")
        mean_in, mean_out = sem("mean_in"), sem("mean_out")
        var_in, var_out = sem("var_in"), sem("var_out")
        gain = sem("gain")
        scaled_v, scaled_a = sem("scaled_v"), sem("scaled_a")
        step = sem("step")
        prod_full, prod_copied = sem("prod_full"), sem("prod_copied")
        turned, stored = sem("turned"), sem("stored")
        block = ctx.enter_context(nc.Block())
        mean, var = statm[:, :, 0], statm[:, :, 1]
        half_images = NB // 2

        @block.sync
        def _(sp):
            for b in range(NB):
                sp.dma_start(raw[:, b, :], spec[b]).then_inc(small_in, 16)
            sp.dma_start(wts[:], wt).then_inc(small_in, 16)
            sp.dma_start(bcol[:], bb[:, None]).then_inc(small_in, 16)
            for k in range(CHUNKS):
                if k >= 2:
                    sp.wait_ge(used, k - 1)
                for high in range(2):
                    for part in range(2):
                        for po in range(2):
                            src = (rre if part == po else rim)[:, :, 16 * high + CH * k:16 * high + CH * (k + 1), :]
                            g = 64 * high + 32 * part
                            sp.dma_start(wmode[k % 2][g:g + 32, 32 * po:32 * po + 32, :],
                                         src.rearrange("i j a b -> j i (a b)")).then_inc(w_full[k % 2], 16)
            for b in range(NB):
                sp.wait_ge(turned, b + 1)
                sp.dma_start(mixed[b], raw[:, b, :]).then_inc(stored, 16)
            sp.wait_ge(stored, 16 * NB)

        @block.gpsimd
        def _(pool):
            nc.gpsimd.memset(moving[0:64, :, NB:2 * NB], 0.0)
            nc.gpsimd.memset(moving[64:128, :, 0:NB], 0.0).then_inc(zeroed, 1)

        @block.tensor
        def _(pe):
            pe.wait_ge(mean_in, 1)
            nc.tensor.matmul(sps[:, 0:NB], con["k_pair"][:], work[:, 3, :], start=True, stop=True).then_inc(mean_out, 1)
            pe.wait_ge(mean_in, 2)
            nc.tensor.matmul(sps[:, NB:2 * NB], con["k_pair"][:], work[:, 0, :], start=True, stop=True).then_inc(mean_out, 1)
            pe.wait_ge(mean_in, 3)
            pe.wait_ge(small_in, 16 * (NB + 2))
            nc.tensor.matmul(sps[0:C, 2 * NB:3 * NB], wts[:], work[0:C, 1, :], start=True, stop=True).then_inc(mean_out, 1)
            pe.wait_ge(scaled_v, 1)
            pe.wait_ge(scaled_a, 1)
            pe.wait_ge(zeroed, 1)
            n = 0
            for k in range(CHUNKS):
                pe.wait_ge(w_full[k % 2], 8 * 16 * (k // 2 + 1))
                pe.wait_ge(w_neg, k + 1)
                for a8 in range(CH // 2):
                    for bh in range(2):
                        if n >= 4:
                            pe.wait_ge(prod_copied, n - 3)
                        for bl in range(16):
                            for odd in range(2):
                                local = (2 * a8 + odd) * MODES + 16 * bh + bl
                                last = nc.tensor.matmul(ps[n % 4][64 * odd:64 * odd + 64, bl * 2 * NB:(bl + 1) * 2 * NB],
                                                        wmode[k % 2][:, :, local], moving[:, k * CM + local, :],
                                                        start=True, stop=True, skip_group_check=True)
                        last.then_inc(prod_full, 1)
                        n += 1
                if k < CHUNKS - 2:
                    pe.wait_ge(prod_full, n)
                    pe.sem_inc(used, 1)

        def scale_images(engine, images, op):
            for b in images:
                for high in range(2):
                    rows = slice(64 * high, 64 * high + 64)
                    last = op(moving[rows, :, high * NB + b], raw[rows, b, :], gscale[rows, b:b + 1])
            return last

        @block.scalar
        def _(act):
            act.wait_ge(var_in, 1)
            nc.scalar.activation(work[:, 4, :], work[:, 2, :], ACT.Sqrt, bias=epst[:]).then_inc(var_out, 1)
            act.wait_ge(small_in, 16 * (NB + 2))
            act.wait_ge(gain, 1)
            scale_images(act, range(half_images, NB),
                         lambda o, i, s: nc.scalar.activation(o, i, ACT.Copy, scale=s)).then_inc(scaled_a, 1)
            n = 0
            for k in range(CHUNKS):
                for a8 in range(CH // 2):
                    for bh in range(2):
                        act.wait_ge(prod_full, n + 1)
                        a = k * (CH // 2) + a8
                        dst = mixd[:, :, :].rearrange("p i (h a b) -> p b h i a", h=2, a=8)[:, 16 * bh:16 * bh + 16, :, :, a]
                        for high in range(2):
                            last = nc.scalar.activation(
                                dst[:, :, high, :],
                                ps[n % 4][:, 0:32 * NB].rearrange("p (b h i) -> p b h i", h=2, i=NB)[:, :, high, :], ACT.Copy)
                        last.then_inc(prod_copied, 1)
                        n += 1

        @block.vector
        def _(dve):
            at = [0]

            def link(ins):
                at[0] += 1
                ins.then_inc(step, 1)
                dve.wait_ge(step, at[0])

            nc.vector.memset(epst[:], EPS)
            link(nc.vector.tensor_copy(work[:, 3, :], mean))
            dve.sem_inc(mean_in, 1)
            dve.wait_ge(mean_out, 1)
            link(nc.vector.tensor_copy(work[:, 5, :], sps[:, 0:NB]))
            link(nc.vector.tensor_tensor(work[:, 0, :], mean, work[:, 5, :], ALU.subtract))
            link(nc.vector.tensor_tensor(work[:, 0, :], work[:, 0, :], work[:, 0, :], ALU.mult))
            link(nc.vector.tensor_tensor(work[:, 0, :], work[:, 0, :], var, ALU.add))
            dve.sem_inc(mean_in, 1)
            dve.wait_ge(mean_out, 2)
            link(nc.vector.tensor_copy(work[:, 2, :], sps[:, NB:2 * NB]))
            dve.sem_inc(var_in, 1)
            dve.wait_ge(var_out, 1)
            link(nc.vector.reciprocal(gscale[:], work[:, 4, :]))
            link(nc.vector.scalar_tensor_tensor(out=work[:, 1, :], in0=work[:, 5, :], scalar=-1.0, in1=gscale[:],
                                                op0=ALU.mult, op1=ALU.mult))
            dve.sem_inc(mean_in, 1)
            dve.sem_inc(gain, 1)
            dve.wait_ge(small_in, 16 * (NB + 2))
            link(scale_images(dve, range(half_images),
                              lambda o, i, s: nc.vector.tensor_scalar(o, i, s, None, ALU.mult)))
            dve.wait_ge(scaled_a, 1)
            link(nc.vector.scalar_tensor_tensor(out=moving[0:32, 0, 0:NB], in0=work[0:32, 1, :], scalar=float(SIZE),
                                                in1=moving[0:32, 0, 0:NB], op0=ALU.mult, op1=ALU.add))
            dve.sem_inc(scaled_v, 1)
            dve.wait_ge(mean_out, 3)
            link(nc.vector.tensor_scalar(wb[:], sps[0:C, 2 * NB:3 * NB], bcol[:], float(SIZE), ALU.add, ALU.mult))
            for k in range(CHUNKS):
                dve.wait_ge(w_full[k % 2], 8 * 16 * (k // 2 + 1))
                for high in range(2):
                    g = 64 * high + 32
                    last = nc.vector.tensor_scalar(wmode[k % 2][g:g + 32, 0:32, :], wmode[k % 2][g:g + 32, 0:32, :],
                                                   -1.0, None, ALU.mult)
                last.then_inc(w_neg, 1)
            dve.wait_ge(prod_copied, 4 * CHUNKS)
            link(nc.vector.tensor_tensor(mixd[0:32, :, 0], mixd[0:32, :, 0], wb[:], ALU.add))
            for b in range(NB):
                nc.vector.transpose(raw[:, b, :], mixd[:, b, :]).then_inc(turned, 1)


def inverse_layer(nc, NB, tag, wt, con, gscale, mixed, src, dst, last_layer, statm=None, spec=None):
    ctx = ExitStack()
    with Semaphores(nc) as sems, ctx:
        def sb(name, shape, dt=f32):
            return ctx.enter_context(nc.sbuf_tensor(tag + name, shape, dt))

        def sem(name):
            return sems.new(tag + name)

        tile = [sb(f"tile{u}", [HR, 2, BANK]) for u in range(TILES)]
        turned = [sb(f"turned{i}", [P, COLS]) for i in range(3)]
        half_inv = [sb(f"half_inv{i}", [P, SIZE, 16]) for i in range(2)]
        spread = [sb(f"spread{i}", [P, 16, P]) for i in range(2)]
        mix_in = sb("mix_in", [P, BANK])
        wblk = sb("wblk", [P, P])
        wnorm = [sb(f"wnorm{i}", [P, P]) for i in range(2)]
        if not last_layer:
            rowspec = sb("rowspec", [P, PAIRS, BANK])
            colspec = sb("colspec", [HR, P, C])
            specout = sb("specout", [P, BANK])
            stat = sb("stat", [P, UNITS, 6])
            aggr = sb("aggr", [P, 2])
            carrier = sb("carrier", [P, 1])
        tps = [ctx.enter_context(nc.psum_tensor(f"{tag}tps{i}", [P, BANK], f32)) for i in range(2)]
        ops = [ctx.enter_context(nc.psum_tensor(f"{tag}ops{i}", [P, BANK], f32)) for i in range(2)]
        sps = [ctx.enter_context(nc.psum_tensor(f"{tag}sps{i}", [P, BANK], f32)) for i in range(2)]
        vps = [ctx.enter_context(nc.psum_tensor(f"{tag}vps{i}", [P, BANK], f32)) for i in range(2)]

        def tps_order(last_image):
            queue = []
            for v in range(UNITS):
                queue.append(("unit", v))
                if v >= 6 and v % 2 == 0 and v < 22 and not last_image:
                    queue.append(("half", (v - 6) // 2))
            if not last_layer:
                queue += [("spec", k) for k in range(8)]
            return queue
        NQ = len(tps_order(False))

        next_seen = sem("next_seen")
        mix_full = sem("mix_full")
        spread_full = sem("spread_full")
        tile_full = [sem(f"tile_full{u}") for u in range(TILES)]
        tile_stored = [sem(f"tile_stored{u}") for u in range(TILES)]
        turn_full = sem("turn_full")
        turn_copied = sem("turn_copied")
        out_full = sem("out_full")
        out_added = sem("out_added")
        next_full = sem("next_full")
        stat_done = sem("stat_done")
        rowspec_full = sem("rowspec_full")
        spec_full = sem("spec_full")
        spec_sb = sem("spec_sb")
        spec_stored = sem("spec_stored")
        wload, setup, step = sem("wload"), sem("setup"), sem("step")
        block = ctx.enter_context(nc.Block())

        @block.sync
        def _(sp):
            sp.sem_inc(spec_stored, 16)
            sp.dma_start(mix_in[:], mixed[0]).then_inc(mix_full, 16)
            for u in range(TILES):
                sp.dma_start(tile[u][:, :, :].rearrange("p s m -> p (s m)"), src[0, u]).then_inc(tile_full[u], 16)

            def body(b, last_image):
                if not last_image:
                    sp.wait_ge(spread_full, b + 1)
                    sp.dma_start(mix_in[:], mixed[bass.ds(b + 1, 1)].rearrange("o p m -> (o p) m")).then_inc(mix_full, 16)
                    for u in range(TILES):
                        if not last_layer:
                            sp.wait_ge(next_full, b * UNITS + 2 * u + 2)
                            sp.sem_inc(next_seen, 1)
                        sp.wait_ge(tile_stored[u], (b + 1) * 16)
                        sp.dma_start(tile[u][:, :, :].rearrange("p s m -> p (s m)"),
                                     src[bass.ds(b + 1, 1), u].rearrange("o p m -> (o p) m")).then_inc(tile_full[u], 16)
                if not last_layer:
                    sp.wait_ge(spec_sb, b + 2)
                    sp.dma_start(spec[bass.ds(b, 1)].rearrange("o p m -> (o p) m"), specout[:]).then_inc(spec_stored, 16)

            with sp.Fori(0, NB - 1) as b:
                body(b, False)
            body(NB - 1, True)
            if not last_layer:
                sp.wait_ge(spec_stored, 16 * NB + 16)

        def half_unit(pe, par, k, dst):
            for i in range(2):
                last = nc.tensor.matmul(dst[:, i * SIZE:(i + 1) * SIZE], spread[par][:, 2 * k + i, :], con["k_dcti"][:],
                                        start=True, stop=True, skip_group_check=True)
            return last

        @block.tensor
        def _(pe):
            pe.sem_inc(out_full, 1)
            pe.wait_ge(spread_full, 1)
            for k in range(8):
                if k >= 2:
                    pe.wait_ge(turn_copied, k - 1)
                half_unit(pe, 0, k, tps[k % 2]).then_inc(turn_full, 1)

            def body(b, par, last_image):
                q0 = 8 + b * NQ
                queue = tps_order(last_image)
                pos = {e: n for n, e in enumerate(queue)}

                def unit_in(v):
                    u, side = divmod(v, 2)
                    if side == 0:
                        pe.wait_ge(tile_full[u], (b + 1) * 16)
                    n = pos["unit", v]
                    pe.wait_ge(turn_copied, q0 + n - 1)
                    for j in range(BLKU):
                        last = nc.tensor.transpose(tps[n % 2][:, j * HR:(j + 1) * HR], tile[u][:, side, j * P:(j + 1) * P],
                                                   con["k_ident"][0:HR, 0:HR])
                    last.then_inc(turn_full, 1)

                def unit_out(v):
                    u, side = divmod(v, 2)
                    half, p = u % 2, u // 2
                    pe.wait_ge(turn_copied, q0 + pos["unit", v] + 1)
                    pe.wait_ge(out_added, b * UNITS + v + 1)
                    dst = ops[v % 2][0:HR, :]
                    for j in range(BLKU):
                        nc.tensor.matmul(dst[:, j * P:(j + 1) * P], turned[v % 3][:, j * HR:(j + 1) * HR], wnorm[par][:],
                                         start=(j == 0), stop=False, skip_group_check=True)
                    q = side * HR + 16 * p
                    for cp in range(2):
                        last = nc.tensor.matmul(dst.rearrange("p (q c) -> p q c", c=C)[:, :, 16 * cp:16 * cp + 16],
                                                con["k_inv"][:, cp, half, :], half_inv[par][:, q:q + 16, :],
                                                start=False, stop=(cp == 1), skip_group_check=True)
                    last.then_inc(out_full, 1)

                def unit_next(v):
                    u, side = divmod(v, 2)
                    half, p = u % 2, u // 2
                    pe.wait_ge(out_added, b * UNITS + v + 1 + 2)
                    if v % 4 == 0:
                        pe.wait_ge(rowspec_full, b * PAIRS + max(p - 1, 0) + 1)
                        if p == 1:
                            pe.wait_ge(spec_sb, b + 1)
                    pe.wait_ge(stat_done, b * UNITS + v + 1)
                    nc.tensor.matmul(vps[p % 2][64 * side:64 * side + 64, :], con["k_fwd"][:, half, :], tile[u][:, side, :],
                                     start=(half == 0), stop=(half == 1), skip_group_check=True)
                    for j in range(BLKU):
                        last = nc.tensor.transpose(sps[v % 2][:, j * HR:(j + 1) * HR], tile[u][:, side, j * P:(j + 1) * P],
                                                   con["k_ident"][0:HR, 0:HR])
                    last.then_inc(next_full, 1)

                for n in range(UNITS + 3):
                    if n < UNITS:
                        unit_in(n)
                        if n % 2 == 0 and ("half", (n - 6) // 2) in pos:
                            m = pos["half", (n - 6) // 2]
                            if n == 6:
                                pe.wait_ge(spread_full, b + 2)
                            pe.wait_ge(turn_copied, q0 + m - 1)
                            half_unit(pe, 1 - par, (n - 6) // 2, tps[m % 2]).then_inc(turn_full, 1)
                    if 1 <= n <= UNITS:
                        unit_out(n - 1)
                    if n >= 3 and not last_layer:
                        unit_next(n - 3)
                if not last_layer:
                    pe.wait_ge(rowspec_full, (b + 1) * PAIRS + 1)
                    rs = rowspec[:, :, :].rearrange("p n (q c) -> p (n q) c", c=C)
                    for k in range(8):
                        m = pos["spec", k]
                        pe.wait_ge(turn_copied, q0 + m - 1)
                        for j in range(4):
                            last = nc.tensor.transpose(tps[m % 2][0:HR, j * P:(j + 1) * P], rs[:, :, 4 * k + j],
                                                       con["k_ident"][:])
                        last.then_inc(turn_full, 1)
                    pe.wait_ge(turn_copied, q0 + len(queue))
                    for side in range(2):
                        for g in range(4):
                            lo = side * KP + 16 * g
                            last = nc.tensor.matmul(vps[1][32 * g:32 * g + 32, :], con["k_dctf"][:, side, :],
                                                    colspec[:, lo:lo + 16, :].rearrange("p k c -> p (k c)"),
                                                    start=(side == 0), stop=(side == 1), skip_group_check=True)
                    last.then_inc(spec_full, 1)

            with pe.Fori(0, NB // 2 - 1) as i:
                body(2 * i, 0, False)
                body(2 * i + 1, 1, False)
            body(NB - 2, 0, False)
            body(NB - 1, 1, True)

        @block.scalar
        def _(act):
            act.sem_inc(rowspec_full, 1)

            def half_copy(par, k, bank):
                nc.scalar.activation(half_inv[par][:, :, 2 * k:2 * k + 2].rearrange("p q c -> p c q"),
                                     bank[:, 0:2 * SIZE].rearrange("p (c q) -> p c q", q=SIZE), ACT.Copy).then_inc(turn_copied, 1)

            for k in range(8):
                act.wait_ge(turn_full, k + 1)
                half_copy(0, k, tps[k % 2])

            def store(b, u):
                act.wait_ge(out_added, b * UNITS + 2 * u + 2 + 2)
                half, p = u % 2, u // 2
                if last_layer:
                    rows = dst[bass.ds(b, 1), half * HR:(half + 1) * HR].rearrange("o r (s q) c -> (o r) s (q c)", s=2)
                    act.dma_start(rows[:, :, 16 * p * C:16 * (p + 1) * C], tile[u][:]).then_inc(tile_stored[u], 16)
                else:
                    act.dma_start(dst[bass.ds(b, 1), u].rearrange("o p m -> (o p) m"),
                                  tile[u][:, :, :].rearrange("p s m -> p (s m)")).then_inc(tile_stored[u], 16)

            def body(b, par, last_image):
                q0 = 8 + b * NQ
                for m, (kind, k) in enumerate(tps_order(last_image)):
                    if kind == "spec" and k == 0:
                        store(b, TILES - 1)
                        rowcopy(b, PAIRS - 1)
                    act.wait_ge(turn_full, q0 + m + 1)
                    bank = tps[m % 2]
                    if kind == "unit":
                        if k >= 3:
                            act.wait_ge(out_full, b * UNITS + k - 1)
                        else:
                            act.wait_ge(out_full, b * UNITS + 1)
                        nc.scalar.activation(turned[k % 3][:], bank[:, 0:COLS], ACT.Copy).then_inc(turn_copied, 1)
                        if k % 2 == 0 and k >= 4:
                            store(b, k // 2 - 2)
                        if k == UNITS - 1:
                            store(b, TILES - 2)
                        if not last_layer and k >= 7 and k % 4 == 3:
                            rowcopy(b, k // 4 - 1)
                    elif kind == "half":
                        half_copy(1 - par, k, bank)
                    else:
                        nc.scalar.activation(colspec[:, :, 4 * k:4 * k + 4].rearrange("p k c -> p c k"),
                                             bank[0:HR, :].rearrange("p (c k) -> p c k", k=P), ACT.Copy).then_inc(turn_copied, 1)
                if last_layer:
                    store(b, TILES - 1)

            def rowcopy(b, p):
                act.wait_ge(next_full, b * UNITS + 4 * (p + 1))
                nc.scalar.activation(rowspec[:, p, :], vps[p % 2][:], ACT.Copy).then_inc(rowspec_full, 1)

            with act.Fori(0, NB // 2 - 1) as i:
                body(2 * i, 0, False)
                body(2 * i + 1, 1, False)
            body(NB - 2, 0, False)
            body(NB - 1, 1, True)
            for u in range(TILES):
                act.wait_ge(tile_stored[u], NB * 16)

        @block.vector
        def _(dve):
            dve.sem_inc(out_added, 2)
            dve.sem_inc(stat_done, 2)
            dve.sem_inc(spec_sb, 1)
            nc.vector.memset(wblk[:], 0.0)
            nc.vector.memset(spread[0][:], 0.0)
            nc.vector.memset(spread[1][:], 0.0).then_inc(setup, 1)
            dve.wait_ge(setup, 1)
            dve.wait_ge(wload, 16 * QG)

            def spread_image(b, par):
                dve.wait_ge(mix_full, (b + 1) * 16)
                for g in range(4):
                    rows = slice(32 * g, 32 * g + 32)
                    nc.vector.tensor_copy(
                        spread[par][rows, :, :].rearrange("p c (h g k) -> p g k h c", h=2, g=4)[:, g],
                        mix_in[rows, :].rearrange("p (k h c) -> p k h c", h=2, c=16))
                col = gscale[:, b:b + 1] if isinstance(b, int) else gscale[:, bass.ds(b, 1)]
                nc.vector.tensor_scalar(wnorm[par][:], wblk[:], col, None, ALU.mult).then_inc(spread_full, 1)

            spread_image(0, 0)

            def body(b, par, last_image):
                for n in range(UNITS + 3):
                    if n < UNITS:
                        u, side = divmod(n, 2)
                        dve.wait_ge(out_full, b * UNITS + n + 2)
                        nc.vector.scalar_tensor_tensor(out=tile[u][:, side, :], in0=ops[n % 2][0:HR, :], scalar=0.0,
                                                       in1=tile[u][:, side, :], op0=ALU.max, op1=ALU.add).then_inc(out_added, 1)
                        if n == 1 and not last_image:
                            spread_image(b + 1, 1 - par)
                    if n >= 3 and not last_layer:
                        v = n - 3
                        dve.wait_ge(next_full, b * UNITS + v + 1)
                        nc.vector.bn_stats(stat[:, v, :], sps[v % 2][:, 0:COLS]).then_inc(stat_done, 1)
                if not last_layer:
                    dve.wait_ge(stat_done, (b + 1) * UNITS + 2)
                    nc.vector.memset(carrier[:], 0.0)
                    nc.vector.bn_aggr(aggr[:], stat[:, :, :].rearrange("p n s -> p (n s)")).then_inc(step, 1)
                    dve.wait_ge(step, b + 1)
                    nc.vector.tensor_copy(statm[:, bass.ds(b, 1), :].rearrange("p o s -> p (o s)"), aggr[:])
                    dve.wait_ge(spec_full, b + 1)
                    dve.wait_ge(spec_stored, b * 16 + 16)
                    nc.vector.transpose(specout[:], vps[1][:]).then_inc(spec_sb, 1)

            with dve.Fori(0, NB // 2 - 1) as i:
                body(2 * i, 0, False)
                body(2 * i + 1, 1, False)
            body(NB - 2, 0, False)
            body(NB - 1, 1, True)

        @block.gpsimd
        def _(pool):
            pool.wait_ge(setup, 1)
            for g in range(QG):
                pool.dma_start(wblk[32 * g:32 * g + 32, 32 * g:32 * g + 32], wt).then_inc(wload, 16)


def program(nc, ins, consts, out):
    NB = ins["x"].shape[0]
    ctx = ExitStack()
    with ctx:
        def sb(name, shape, dt):
            return ctx.enter_context(nc.sbuf_tensor(name, shape, dt))

        statm = sb("statm", [P, NB, 2], f32)
        gscale = sb("gscale", [P, NB], f32)
        xpad = nc.dram_tensor("xpad", [29 + HR, SIZE, C], f32).ap()
        spec = nc.dram_tensor("spec", [NB, P, BANK], f32).ap()
        mixed = nc.dram_tensor("mixed", [NB, P, BANK], f32).ap()
        x2s = nc.dram_tensor("x2s", [NB, TILES, HR, 2 * BANK], f32).ap()
        x3s = nc.dram_tensor("x3s", [NB, TILES, HR, 2 * BANK], f32).ap()

        def phase(tag, names, run):
            with ExitStack() as inner:
                con = load_constants(nc, lambda n, s, d: inner.enter_context(nc.sbuf_tensor(n, s, d)), tag,
                                     {n: (consts[n], list(consts[n].shape)) for n in names})
                run(con)

        phase("a_", ["k_fwd", "k_dctf", "k_ident", "k_pair", "k_pairn", "k_same", "k_rows", "k_cols"],
              lambda con: shift_conv_forward(nc, NB, ins["x"], ins["L1_conv_W"], ins["L1_conv_b"], ins["L0_conv_W"],
                                             ins["L0_conv_b"], con, statm, xpad, x2s, spec))
        for layer, tag, src, dst, last in (("L2_conv_", "B_", x2s, x3s, False), ("L3_conv_", "C_", x3s, out, True)):
            phase("m" + tag, ["k_pair"],
                  lambda con: mix_modes(nc, NB, ins[layer + "R_real"], ins[layer + "R_imag"], ins[layer + "W"],
                                        ins[layer + "b"], con, statm, gscale, spec, mixed, tag))
            phase("i" + tag, ["k_ident", "k_inv", "k_dcti"] + ([] if last else ["k_fwd", "k_dctf"]),
                  lambda con: inverse_layer(nc, NB, tag, ins[layer + "W"], con, gscale, mixed, src, dst, last, statm, spec))


_INS = ["x", "L0_conv_W", "L0_conv_b", "L1_conv_W", "L1_conv_b", "L2_conv_R_real", "L2_conv_R_imag", "L2_conv_W",
        "L2_conv_b", "L3_conv_R_real", "L3_conv_R_imag", "L3_conv_W", "L3_conv_b"]


def kernel(**inputs):
    import concourse.bacc as bacc
    from concourse.bass_utils import run_bass_kernel_spmd

    nc = bacc.Bacc("TRN2", target_bir_lowering=False, num_devices=1)
    arrays, ins, consts = {}, {}, {}
    for name in _INS:
        a = np.asarray(inputs[name])
        a = np.ascontiguousarray(a.T if name in ("L2_conv_W", "L3_conv_W") else a)
        arrays[f"in_{name}"] = a
        ins[name] = nc.dram_tensor(f"in_{name}", a.shape, mybir.dt.from_np(a.dtype), kind="ExternalInput").ap()
    for name, a in constants().items():
        arrays[name] = a
        consts[name] = nc.dram_tensor(name, a.shape, f32, kind="ExternalInput").ap()
    out = nc.dram_tensor("out_0", arrays["in_x"].shape, f32, kind="ExternalOutput").ap()
    program(nc, ins, consts, out)
    r = run_bass_kernel_spmd(nc, [arrays], core_ids=[0])
    return r.results[0]["out_0"]
```
